# Optimizing a Trainium2 kernel written in Bass

```python
import numpy as np
import jax
import jax.numpy as jnp

def _softmax(x, axis=-1):
    return jax.nn.softmax(x, axis=axis)

def _gelu(x):
    return jax.nn.gelu(x, approximate=True)

def _silu(x):
    return jax.nn.silu(x)

def _sigmoid(x):
    return jax.nn.sigmoid(x)

def _layernorm(x, axis=-1, eps=1e-05):
    m = jnp.mean(x, axis=axis, keepdims=True)
    v = jnp.var(x, axis=axis, keepdims=True)
    return (x - m) / jnp.sqrt(v + eps)

def _scatter_add(tgt, idx, src, axis=0):
    return tgt.at[idx].add(src)

def _segment_sum(src, seg, n):
    return jax.ops.segment_sum(src, seg, n)
kernel_name = 'mk_adaln_d1_jaxref_r4_23281b'

def setup_inputs(seed: int=0):
    np.random.seed(seed)
    _w = jnp.asarray

    def _L0_attn_setup():
        import jax, jax.numpy as jnp
        import numpy as np
        B, T, C = (64, 64, 256)
        N_HEAD, HEAD_SIZE, KV_RANK = (16, 64, 128)
        BLOCK_SIZE = 64
        key = jax.random.key(seed)
        ks = jax.random.split(key, 5)
        HD = N_HEAD * HEAD_SIZE

        def init(k, shape):
            fan_in = shape[0]
            bound = 1.0 / np.sqrt(fan_in)
            return jax.random.uniform(k, shape, jnp.float32, -bound, bound)
        return {'x': jax.random.normal(ks[0], (B, T, C), jnp.float32), 'w_kv_down': init(ks[1], (C, KV_RANK)), 'w_kv_up': init(ks[2], (KV_RANK, 2 * HD)), 'w_q': init(ks[3], (C, HD)), 'w_out': init(ks[4], (HD, C))}
    _L0_attn_in = _L0_attn_setup()

    def _L0_ffn_setup():
        import jax, jax.numpy as jnp
        import numpy as np
        E, K, D, F = (8, 2, 256, 1024)
        EPS = 1e-06
        B, S = (2, 256)
        key = jax.random.key(seed)
        ks = jax.random.split(key, 6)
        s_in = 1.0 / np.sqrt(D)
        s_mid = 1.0 / np.sqrt(F)
        return {'x': jax.random.normal(ks[0], (B, S, D), dtype=jnp.float32), 'Wg': jax.random.normal(ks[1], (D, E), dtype=jnp.float32) * s_in, 'gamma': jnp.ones((E, D), dtype=jnp.float32), 'beta': jnp.zeros((E, D), dtype=jnp.float32), 'W1': jax.random.normal(ks[2], (E, D, F), dtype=jnp.float32) * s_in, 'b1': jnp.zeros((E, F), dtype=jnp.float32), 'W2': jax.random.normal(ks[3], (E, F, D), dtype=jnp.float32) * s_mid, 'b2': jnp.zeros((E, D), dtype=jnp.float32)}
    _L0_ffn_in = _L0_ffn_setup()
    _L0_c = _w((lambda *s: np.random.randn(*s).astype(np.float32) * 0.05)(4, 256))
    _L0_wmod = _w((lambda *s: np.random.randn(*s).astype(np.float32) * 0.05)(256, 6 * 256) * 256 ** (-0.5))
    _d = {'L0_attn_x': _L0_attn_in['x'], 'L0_attn_w_kv_down': _L0_attn_in['w_kv_down'], 'L0_attn_w_kv_up': _L0_attn_in['w_kv_up'], 'L0_attn_w_q': _L0_attn_in['w_q'], 'L0_attn_w_out': _L0_attn_in['w_out'], 'L0_ffn_Wg': _L0_ffn_in['Wg'], 'L0_ffn_gamma': _L0_ffn_in['gamma'], 'L0_ffn_beta': _L0_ffn_in['beta'], 'L0_ffn_W1': _L0_ffn_in['W1'], 'L0_ffn_b1': _L0_ffn_in['b1'], 'L0_ffn_W2': _L0_ffn_in['W2'], 'L0_ffn_b2': _L0_ffn_in['b2'], 'L0_c': _L0_c, 'L0_wmod': _L0_wmod}
    _x0 = _d['L0_attn_x']
    _d['L0_attn_x'] = jax.random.normal(jax.random.fold_in(jax.random.key(seed), 1), (4, 1024, 256), dtype=_x0.dtype)
    del _x0
    return _d

def reference(L0_attn_x, L0_attn_w_kv_down, L0_attn_w_kv_up, L0_attn_w_q, L0_attn_w_out, L0_ffn_Wg, L0_ffn_gamma, L0_ffn_beta, L0_ffn_W1, L0_ffn_b1, L0_ffn_W2, L0_ffn_b2, L0_c, L0_wmod):

    def _L0_attn_ref(x, w_kv_down, w_kv_up, w_q, w_out):
        import jax, jax.numpy as jnp
        import numpy as np
        B, T, C = (64, 64, 256)
        N_HEAD, HEAD_SIZE, KV_RANK = (16, 64, 128)
        BLOCK_SIZE = 64
        Bx, Tx, Cx = x.shape
        HD = N_HEAD * HEAD_SIZE
        latent_kv = x @ w_kv_down
        kv = latent_kv @ w_kv_up
        k, v = (kv[..., :HD], kv[..., HD:])
        k = k.reshape(Bx, Tx, N_HEAD, HEAD_SIZE)
        v = v.reshape(Bx, Tx, N_HEAD, HEAD_SIZE)
        q = (x @ w_q).reshape(Bx, Tx, N_HEAD, HEAD_SIZE)
        scale = HEAD_SIZE ** (-0.5)
        att = jnp.einsum('bqhd,bkhd->bhqk', q, k) * scale
        causal = jnp.tril(jnp.ones((Tx, Tx), dtype=bool))
        att = jnp.where(causal, att, -jnp.inf)
        att = jax.nn.softmax(att, axis=-1)
        y = jnp.einsum('bhqk,bkhd->bqhd', att, v)
        y = y.reshape(Bx, Tx, HD)
        return y @ w_out

    def _L0_ffn_ref(x, Wg, gamma, beta, W1, b1, W2, b2):
        import jax, jax.numpy as jnp
        import numpy as np
        E, K, D, F = (8, 2, 256, 1024)
        EPS = 1e-06
        B, S = (2, 256)
        orig_shape = x.shape
        xf = x.reshape(-1, orig_shape[-1])
        scores = xf @ Wg
        w, idx = jax.lax.top_k(scores, K)
        w = jax.nn.softmax(w, axis=-1)
        mu = jnp.mean(xf, axis=-1, keepdims=True)
        var = jnp.var(xf, axis=-1, keepdims=True)
        xhat = (xf - mu) * jax.lax.rsqrt(var + EPS)
        normed = xhat[None, :, :] * gamma[:, None, :] + beta[:, None, :]
        h = jax.nn.relu(jnp.einsum('end,edf->enf', normed, W1) + b1[:, None, :])
        out = jnp.einsum('enf,efd->end', h, W2) + b2[:, None, :] + xf[None, :, :]
        cw = jnp.sum(w[..., None] * jax.nn.one_hot(idx, E, dtype=w.dtype), axis=1)
        y = jnp.einsum('ne,end->nd', cw, out)
        return y.reshape(orig_shape)
    x = L0_attn_x
    mod = (_silu(L0_c) @ L0_wmod).reshape(L0_c.shape[0], 6, 1, -1)
    sa, ca, ga, sb, cb, gb = (mod[:, 0], mod[:, 1], mod[:, 2], mod[:, 3], mod[:, 4], mod[:, 5])
    ga = (2 * (ga >= 0) - 1) * jnp.maximum(jnp.abs(ga), 0.25)
    gb = (2 * (gb >= 0) - 1) * jnp.maximum(jnp.abs(gb), 0.25)
    h = _layernorm(x, axis=-1) * (1 + ca) + sa
    x = x + ga * _L0_attn_ref(h, L0_attn_w_kv_down, L0_attn_w_kv_up, L0_attn_w_q, L0_attn_w_out)
    h = _layernorm(x, axis=-1) * (1 + cb) + sb
    x = x + gb * _L0_ffn_ref(h, L0_ffn_Wg, L0_ffn_gamma, L0_ffn_beta, L0_ffn_W1, L0_ffn_b1, L0_ffn_W2, L0_ffn_b2)
    return x

_drawn_inputs = setup_inputs


def setup_inputs(seed=0):
    import zlib

    import numpy as np

    out = dict(_drawn_inputs(seed))
    spreads = {'L0_ffn_gamma': (1.0, 0.6),
     'L0_ffn_beta': (0.0, 2.0),
     'L0_ffn_b1': (0.0, 2.0),
     'L0_ffn_b2': (0.0, 2.0)}
    factors = {'L0_attn_w_kv_down': 8.0,
     'L0_attn_w_kv_up': 8.0,
     'L0_attn_w_q': 8.0,
     'L0_attn_w_out': 8.0,
     'L0_ffn_Wg': 6.883,
     'L0_ffn_W1': 8.0,
     'L0_ffn_W2': 6.395}
    for name, (base, spread) in spreads.items():
        noise = np.random.default_rng([zlib.crc32(name.encode()), seed]).standard_normal(out[name].shape)
        drawn = base * np.exp(spread * noise) if base else spread * noise
        out[name] = jnp.asarray(drawn.astype(out[name].dtype))
    for name, factor in factors.items():
        out[name] = (out[name] * factor).astype(out[name].dtype)
    return out
```

```python
from contextlib import ExitStack

import concourse.bass as bass
from concourse import mybir

ALU = mybir.AluOpType
ACT = mybir.ActivationFunctionType
AX_X = mybir.AxisListType.X
F32 = mybir.dt.float32
F32R = mybir.dt.float32r
BF16 = mybir.dt.bfloat16
I32 = mybir.dt.int32
U32 = mybir.dt.uint32
ds = bass.ds

P = 128
B, T, C = 4, 1024, 256
H, D = 16, 64
HD = H * D
R = 128
E, TOP, F = 8, 2, 1024
N = B * T
TILES = N // P
G = 4
GROUPS = TILES // G
GB = T // (G * P)
KC = C // P
FC = F // P
QT = T // P
PAIRS = H // 2
NP = B * PAIRS
SCALE = float(D) ** -0.5
EPS_LN = 1e-5
EPS_FFN = 1e-6
MASKED = -1e30
REGION = N + P
ET = (N * TOP) // P + E
ETP = ET
CH = 2 * E * KC + E * FC + B * KC
DMA = 16


def need(eng, sem, value):
    if isinstance(value, int) and value <= 0:
        return
    eng.wait_ge(sem, value)


def held(eng, sem, value, spot):
    need(eng, sem, value)
    if not isinstance(value, int):
        eng.memset(spot, 0.0)


def rounds(eng, body, count):
    body(0)
    with eng.Fori(1, count) as i:
        body(i)


class Tally:

    def __init__(self, sem, i, per):
        self.sem, self.base, self.per, self.k = sem, i * per, per, 0

    def inc(self, ins):
        ins.then_inc(self.sem, 1)
        self.k += 1
        assert self.k <= self.per
        return self.base + self.k


def over(ap, axis, count):
    ap = ap.unsqueeze(axis)
    shape = list(ap.shape)
    shape[axis] = count
    return ap.broadcast_to(shape)


def chunks(i):
    width = P * (i + 1)
    out = []
    at = 0
    while at < width:
        w = min(512, max(256, width - at))
        out.append((at, w))
        at += w
    return out


def block_kernel(nc, x, wkd, wku, wq, wo, wg, gamma, beta, w1, b1, w2, b2, c, wmod, out):
    top = ExitStack()
    with top:
        def sb(name, shape, dt=F32, ctx=top):
            return ctx.enter_context(nc.sbuf_tensor(name, shape, dt))

        def ps(name, cols, ctx):
            return ctx.enter_context(nc.psum_tensor(name, [P, cols], F32))

        def sem(name):
            return top.enter_context(nc.semaphore(name))

        xf = x.rearrange("b t c -> (b t) c")
        outf = out.rearrange("b t c -> (b t) c")

        def dram(name, shape):
            return nc.dram_tensor(name, shape, F32, kind="Internal").ap()

        mod_d = dram("mod_rows", [B, 6 * C])
        v_d = dram("values", [N, HD])
        y_d = dram("attended", [NP, P, T])
        x1_d = dram("x_after_attention", [N, C])
        h2_d = dram("ffn_input", [N, C])
        rows_d = dram("expert_rows", [E * REGION, C])
        eo_d = dram("expert_out", [ET * P, C])

        ident = sb("ident", [P, P])
        before_me = sb("before_me", [P, P], BF16)
        ones_bf = sb("ones_bf", [P, P], BF16)
        causal = sb("causal", [P, T])
        zeros = sb("zeros", [P, C])
        mhalf = sb("mhalf", [P, G])
        tri8 = sb("tri8", [P, E, E])
        ints = sb("ints", [P, 8 + 8 + 1 + ET + 32], I32)
        flts = sb("flts", [P, 8 + 8 + 1 + ET + 32])
        iota_e = flts[:, 0:8]
        base_e = flts[:, 8:16]
        part = flts[:, 16:17]
        iota_t = flts[:, 17:17 + ET]
        steps = flts[:, 17 + ET:17 + ET + 32]
        mod_cols = sb("mod_cols", [P, 2, KC, B])
        mod_bc = sb("mod_bc", [P, B, 4, C])
        counts = sb("counts", [P, E], BF16)
        best = sb("best", [P, TILES, TOP])
        chosen = sb("chosen", [P, TILES, TOP, E])
        place = sb("place", [P, TILES, TOP])
        gate = sb("gate", [P, TILES, TOP + 1])
        plan_e = sb("plan_e", [P, ET], I32)
        plan_r = sb("plan_r", [P, ET], I32)
        gather_at = sb("gather_at", [P, TILES * TOP], U32)
        channels = sb("channels", [P, CH])
        norm_g = channels[:, 0:E * KC].rearrange("p (e k) -> p e k", k=KC)
        norm_b = channels[:, E * KC:2 * E * KC].rearrange("p (e k) -> p e k", k=KC)
        bias1 = channels[:, 2 * E * KC:2 * E * KC + E * FC].rearrange("p (e f) -> p e f", f=FC)

        setup(nc, sb, ps, sem, locals())
        with ExitStack() as mem:
            hT = sb("hT", [P, KC, N], ctx=mem)
            latT = sb("latT", [P, N], ctx=mem)
            before(nc, sb, ps, sem, xf, wkd, wku, v_d, hT, latT, ident, mhalf, mod_cols)
            attend(nc, sb, ps, sem, wq, wku, v_d, y_d, hT, latT, ident, causal)
        with ExitStack() as mem:
            w_all = sb("w_all", [P, E, KC * F + FC * C], ctx=mem)
            w_in = sem("w_in")
            after(nc, sb, ps, sem, xf, y_d, wo, wg, w1, w2, w_all, w_in, x1_d, h2_d, rows_d,
                  ident, mhalf, before_me, ones_bf, iota_e, base_e, mod_bc, counts, best, chosen,
                  place)
            plan(nc, sb, ps, sem, rows_d, ones_bf, counts, zeros, base_e, part, iota_t, steps,
                 tri8, best, chosen, place, gate, plan_e, plan_r, gather_at)
            experts(nc, sb, ps, sem, w_all, w_in, rows_d, eo_d, b2, ident, bias1, norm_g, norm_b,
                    plan_e, plan_r)
        combine(nc, sb, sem, eo_d, x1_d, h2_d, outf, mod_bc, gate, gather_at)


def setup(nc, sb, ps, sem, v):
    with ExitStack() as mem:
        flat = sb("flat", [CH, P], ctx=mem)
        eT = sb("eT", [P, B * KC], ctx=mem)
        dT = sb("dT", [P, B * KC], ctx=mem)
        qT = sb("qT", [P, B * KC], ctx=mem)
        silu = sb("silu", [P, B, KC], ctx=mem)
        cT = v["channels"][:, CH - B * KC:CH]
        wm = sb("wm", [P, KC, 6 * C], ctx=mem)
        rows = sb("rows", [B, 6 * C], ctx=mem)
        mag = sb("mag", [B, 2, C], ctx=mem)
        mag2 = sb("mag2", [B, 2, C], ctx=mem)
        sgn = sb("sgn", [B, 2, C], ctx=mem)
        p_cols = ps("p_cols", 512, mem)
        p_rows = ps("p_rows", 3 * 512, mem)
        s_load = sem("s_load")
        s_small = sem("s_small")
        s_const = sem("s_const")
        s_exp = sem("s_exp")
        s_silu = sem("s_silu")
        s_flat = sem("s_flat")
        s_channels = sem("s_channels")
        s_cols = sem("s_cols")
        s_rows = sem("s_rows")
        s_link = sem("s_link")
        s_rowsdone = sem("s_rowsdone")
        s_rowsout = sem("s_rowsout")
        s_bc = sem("s_bc")

        with nc.Block() as block:
            @block.sync
            def _(sp):
                at = 0
                for src, q in ((v["gamma"], P), (v["beta"], P), (v["b1"], P), (v["c"], P)):
                    n = src.shape[0] * src.shape[1] // q
                    sp.dma_start(flat[at:at + n, :], src.rearrange("r (k p) -> (r k) p", p=q)).then_inc(s_small, DMA)
                    at += n
                sp.dma_start(wm[:, :, :], v["wmod"].rearrange("(k p) n -> p k n", p=P)).then_inc(s_load, DMA)
                sp.wait_ge(s_rowsdone, 1)
                sp.dma_start(v["mod_d"][:, :], rows[:, :]).then_inc(s_rowsout, DMA)
                sp.wait_ge(s_rowsout, DMA)
                for b in range(B):
                    sp.dma_start(v["mod_bc"][:, b, :, :].rearrange("p a c -> p (a c)"),
                                 v["mod_d"][b, 2 * C:6 * C].partition_broadcast(P)).then_inc(s_bc, DMA)
                sp.wait_ge(s_bc, B * DMA)

            @block.gpsimd
            def _(pool):
                pool.memset(v["ident"][:, :], 0.0).then_inc(s_const, 1)
                pool.memset(v["before_me"][:, :], 1.0).then_inc(s_const, 1)
                pool.memset(v["ones_bf"][:, :], 1.0).then_inc(s_const, 1)
                pool.memset(v["causal"][:, :], 0.0).then_inc(s_const, 1)
                pool.memset(v["zeros"][:, :], 0.0).then_inc(s_const, 1)
                pool.memset(v["mhalf"][:, :], -0.5).then_inc(s_const, 1)
                pool.memset(v["tri8"][:, :, :], 1.0).then_inc(s_const, 1)
                pool.memset(v["counts"][:, :], 0.0).then_inc(s_const, 1)
                ints = v["ints"]
                pool.iota(ints[:, 0:8], pattern=[[1, 8]], base=0, channel_multiplier=0).then_inc(s_const, 1)
                pool.iota(ints[:, 8:16], pattern=[[REGION, 8]], base=0, channel_multiplier=0).then_inc(s_const, 1)
                pool.iota(ints[:, 16:17], pattern=[[1, 1]], base=0, channel_multiplier=1).then_inc(s_const, 1)
                pool.iota(ints[:, 17:17 + ET], pattern=[[1, ET]], base=0, channel_multiplier=0).then_inc(s_const, 1)
                pool.iota(ints[:, 17 + ET:17 + ET + 32], pattern=[[P, 32]], base=0, channel_multiplier=0).then_inc(s_const, 1)
                pool.wait_ge(s_const, 13)
                pool.affine_select(out=v["ident"][:, :], in_=v["ident"][:, :], compare_op=ALU.not_equal,
                                   fill=1.0, base=0, pattern=[[-1, P]], channel_multiplier=1).then_inc(s_const, 1)
                pool.affine_select(out=v["before_me"][:, :], in_=v["before_me"][:, :], compare_op=ALU.is_gt,
                                   fill=0.0, base=0, pattern=[[1, P]], channel_multiplier=-1).then_inc(s_const, 1)
                pool.affine_select(out=v["causal"][:, T - P:T], in_=v["causal"][:, T - P:T], compare_op=ALU.is_ge,
                                   fill=MASKED, base=0, pattern=[[-1, P]], channel_multiplier=1).then_inc(s_const, 1)
                pool.affine_select(out=v["tri8"][:, :, :], in_=v["tri8"][:, :, :], compare_op=ALU.is_ge,
                                   fill=0.0, base=0, pattern=[[1, E], [-1, E]], channel_multiplier=0).then_inc(s_const, 1)

            @block.scalar
            def _(act):
                act.wait_ge(s_channels, 1)
                act.activation(eT[:, :], cT, ACT.Exp, scale=-1.0).then_inc(s_exp, 1)

            @block.tensor
            def _(pe):
                pe.wait_ge(s_small, 4 * DMA)
                pe.wait_ge(s_const, 14)
                pe.transpose(p_cols[:, 0:CH], flat[:, :], v["ident"][0:CH, 0:CH]).then_inc(s_flat, 1)
                pe.wait_ge(s_load, DMA)
                pe.wait_ge(s_silu, 1)
                for w in range(2):
                    for cc in range(KC):
                        col = (w * KC + cc) * B
                        for k in range(KC):
                            mm = pe.matmul(p_cols[:, col:col + B], wm[:, k, w * C + cc * P:w * C + (cc + 1) * P],
                                           silu[:, :, k], start=(k == 0), stop=(k == KC - 1))
                mm.then_inc(s_cols, 1)
                for r in range(3):
                    for k in range(KC):
                        mm = pe.matmul(p_rows[0:B, r * 512:(r + 1) * 512], silu[:, :, k],
                                       wm[:, k, r * 512:(r + 1) * 512], start=(k == 0), stop=(k == KC - 1))
                mm.then_inc(s_rows, 1)

            @block.vector
            def _(dve):
                link = Tally(s_link, 0, 99)
                dve.wait_ge(s_flat, 1)
                dve.tensor_copy(v["channels"][:, :], p_cols[:, 0:CH]).then_inc(s_channels, 1)
                dve.wait_ge(s_exp, 1)
                dve.wait_ge(s_link, link.inc(dve.tensor_scalar(dT[:, :], eT[:, :], 1.0, None, ALU.add)))
                dve.wait_ge(s_link, link.inc(dve.reciprocal(qT[:, :], dT[:, :])))
                dve.tensor_tensor(silu[:, :, :].rearrange("p b k -> p (b k)"), cT, qT[:, :], ALU.mult).then_inc(s_silu, 1)
                dve.wait_ge(s_const, 13)
                dve.tensor_copy(v["flts"][:, :], v["ints"][:, :]).then_inc(s_link, 1)
                link.k += 1
                dve.wait_ge(s_cols, 1)
                cols = v["mod_cols"].ap().rearrange("p w k b -> p (w k b)")
                dve.tensor_copy(cols[:, 0:KC * B], p_cols[:, 0:KC * B]).then_inc(s_link, 1)
                link.k += 1
                dve.tensor_scalar(cols[:, KC * B:], p_cols[:, KC * B:2 * KC * B], 1.0, None, ALU.add).then_inc(s_link, 1)
                link.k += 1
                dve.wait_ge(s_rows, 1)
                dve.wait_ge(s_link, link.inc(dve.tensor_copy(rows[:, :], p_rows[0:B, :])))
                for n, w in enumerate((2, 5)):
                    g = rows[:, w * C:(w + 1) * C]
                    dve.wait_ge(s_link, link.inc(dve.scalar_tensor_tensor(
                        out=mag[:, n, :], in0=g, scalar=-1.0, in1=g, op0=ALU.mult, op1=ALU.max)))
                    dve.wait_ge(s_link, link.inc(dve.tensor_scalar(mag2[:, n, :], mag[:, n, :], 0.25, None, ALU.max)))
                    dve.wait_ge(s_link, link.inc(dve.tensor_scalar(sgn[:, n, :], g, 0.0, 2.0, ALU.is_ge, ALU.mult)))
                    dve.wait_ge(s_link, link.inc(dve.scalar_tensor_tensor(
                        out=g, in0=sgn[:, n, :], scalar=-1.0, in1=mag2[:, n, :], op0=ALU.add, op1=ALU.mult)))
                g = rows[:, 4 * C:5 * C]
                dve.tensor_scalar(g, g, 1.0, None, ALU.add).then_inc(s_rowsdone, 1)


def before(nc, sb, ps, sem, xf, wkd, wku, v_d, hT, latT, ident, mhalf, mod_cols):
    with ExitStack() as mem:
        xt = sb("b_x", [P, G, C], ctx=mem)
        xh = sb("b_xhat", [P, G, C], ctx=mem)
        st = sb("b_stats", [P, G, 6], ctx=mem)
        mv = sb("b_mv", [P, G, 2], ctx=mem)
        ve = sb("b_ve", [P, G], ctx=mem)
        rstd = sb("b_rstd", [P, G], ctx=mem)
        spot = sb("b_spot", [P, 1], ctx=mem)
        w_kd = sb("b_wkd", [P, KC, R], ctx=mem)
        w_v = sb("b_wv", [R, HD], ctx=mem)
        lat = sb("b_lat", [P, G * P], ctx=mem)
        vt = sb("b_v", [P, 2, HD], ctx=mem)
        p_x = ps("b_px", KC * 512, mem)
        p_l = ps("b_pl", 512, mem)
        p_v = [ps(f"b_pv{k}", HD, mem) for k in range(2)]
        w_in = sem("b_w_in")
        x_in = sem("b_x_in")
        stats = sem("b_stats_done")
        var_ready = sem("b_var_ready")
        rstd_ready = sem("b_rstd_ready")
        xhat_done = sem("b_xhat_done")
        xT_done = sem("b_xT_done")
        h_done = sem("b_h_done")
        lat_done = sem("b_lat_done")
        lat_copied = sem("b_lat_copied")
        latT_done = sem("b_latT_done")
        v_done = sem("b_v_done")
        v_lo = sem("b_v_lo")
        v_hi = sem("b_v_hi")
        v_out = [sem(f"b_v_out{k}") for k in range(2)]

        with nc.Block() as block:
            @block.sync
            def _(sp):
                sp.dma_start(w_kd[:, :, :], wkd.rearrange("(k p) n -> p k n", p=P)).then_inc(w_in, DMA)
                sp.dma_start(w_v[:, :], wku[:, HD:2 * HD]).then_inc(w_in, DMA)

                def load(g):
                    need(sp, xhat_done, G * g)
                    sp.dma_start(xt[:, :, :], xf[ds(g * (G * P), G * P), :].rearrange("(j p) c -> p j c", p=P)).then_inc(x_in, DMA)

                def store(g):
                    for j in range(G):
                        k = j % 2
                        sp.wait_ge(v_lo, G * g + j + 1)
                        sp.wait_ge(v_hi, G * g + j + 1)
                        sp.dma_start(v_d[ds((g * G + j) * P, P), :], vt[:, k, :]).then_inc(v_out[k], DMA)

                load(0)
                with sp.Fori(0, GROUPS - 1) as g:
                    load(g + 1)
                    store(g)
                store(GROUPS - 1)
                for k in range(2):
                    sp.wait_ge(v_out[k], DMA * TILES // 2)

            @block.gpsimd
            def _(pool):
                def body(g):
                    pool.wait_ge(var_ready, g + 1)
                    pool.tensor_tensor(rstd[:, :], ve[:, :], mhalf[:, :], ALU.pow).then_inc(rstd_ready, 1)
                rounds(pool, body, GROUPS)

            @block.vector
            def _(dve):
                def norm_stats(g):
                    done = Tally(stats, g, 2 * G)
                    dve.wait_ge(x_in, DMA * (g + 1))
                    for j in range(G):
                        at = done.inc(dve.bn_stats(st[:, j, :], xt[:, j, :]))
                    held(dve, stats, at, spot[:, :])
                    for j in range(G):
                        at = done.inc(dve.bn_aggr(mv[:, j, :], st[:, j, :]))
                    dve.wait_ge(stats, at)
                    dve.tensor_scalar(ve[:, :], mv[:, :, 1], EPS_LN, None, ALU.add).then_inc(var_ready, 1)

                def norm(g):
                    dve.wait_ge(rstd_ready, g + 1)
                    need(dve, xT_done, g)
                    for j in range(G):
                        dve.tensor_scalar(xh[:, j, :], xt[:, j, :], mv[:, j, 0:1], rstd[:, j:j + 1],
                                          ALU.subtract, ALU.mult).then_inc(xhat_done, 1)

                def body(g):
                    last = isinstance(g, int) and g == GROUPS - 1
                    dve.wait_ge(lat_done, g + 1)
                    need(dve, v_done, G * g)
                    need(dve, latT_done, g)
                    dve.tensor_copy(lat[:, :], p_l[:, :]).then_inc(lat_copied, 1)
                    if not last:
                        norm_stats(g + 1)
                    for j in range(G):
                        k = j % 2
                        dve.wait_ge(v_done, G * g + j + 1)
                        need(dve, v_out[k], DMA * (2 * g + j // 2))
                        dve.tensor_copy(vt[:, k, 0:512], p_v[k][:, 0:512]).then_inc(v_lo, 1)
                        if j == 1 and not last:
                            norm(g + 1)

                norm_stats(0)
                norm(0)
                rounds(dve, body, GROUPS - 1)
                body(GROUPS - 1)

            @block.tensor
            def _(pe):
                pe.wait_ge(w_in, 2 * DMA)

                def body(g):
                    need(pe, h_done, KC * g)
                    for j in range(G):
                        pe.wait_ge(xhat_done, G * g + j + 1)
                        for k in range(KC):
                            mm = pe.transpose(p_x[:, k * 512 + j * P:k * 512 + (j + 1) * P],
                                              xh[:, j, k * P:(k + 1) * P], ident[:, :])
                    mm.then_inc(xT_done, 1)
                    pe.wait_ge(h_done, KC * g + KC)
                    for k in range(KC):
                        mm = pe.matmul(p_l[:, :], w_kd[:, k, :], hT[:, k, ds(g * (G * P), G * P)],
                                       start=(k == 0), stop=(k == KC - 1))
                    mm.then_inc(lat_done, 1)
                    pe.wait_ge(lat_copied, g + 1)
                    for j in range(G):
                        k = j % 2
                        need(pe, v_lo, G * g + j - 1)
                        need(pe, v_hi, G * g + j - 1)
                        for h in range(2):
                            mm = pe.matmul(p_v[k][:, h * 512:(h + 1) * 512], lat[:, j * P:(j + 1) * P],
                                           w_v[:, h * 512:(h + 1) * 512], start=True, stop=True)
                        mm.then_inc(v_done, 1)
                rounds(pe, body, GROUPS)

            @block.scalar
            def _(act):
                def body(g):
                    act.wait_ge(xT_done, g + 1)
                    b = g // GB
                    for k in range(KC):
                        act.activation(hT[:, k, ds(g * (G * P), G * P)], p_x[:, k * 512:(k + 1) * 512], ACT.Identity,
                                       scale=mod_cols[:, 1, k, ds(b, 1)], bias=mod_cols[:, 0, k, ds(b, 1)]).then_inc(h_done, 1)
                    act.wait_ge(lat_copied, g + 1)
                    act.copy(latT[:, ds(g * (G * P), G * P)], lat[:, :]).then_inc(latT_done, 1)
                    for j in range(G):
                        k = j % 2
                        act.wait_ge(v_done, G * g + j + 1)
                        need(act, v_out[k], DMA * (2 * g + j // 2))
                        act.copy(vt[:, k, 512:HD], p_v[k][:, 512:HD]).then_inc(v_hi, 1)
                rounds(act, body, GROUPS)


UNITS = 2 * QT
BLOCKS = [u // 2 + 1 for u in range(UNITS)]
ROUNDS = [(n + 3) // 4 for n in BLOCKS]
FIRST_ROUND = [sum(ROUNDS[:u]) for u in range(UNITS + 1)]
NR = FIRST_ROUND[UNITS]
assert GROUPS == E
LAG = 3
PROJECT_AT = (2, 4, 6, 8)


def attend(nc, sb, ps, sem, wq, wku, v_d, y_d, hT, latT, ident, causal):
    with ExitStack() as mem:
        q_s = [sb(f"a_q{k}", [P, 2, T], F32R, ctx=mem) for k in range(2)]
        k_a = [sb(f"a_ka{k}", [P, 2, T], F32R, ctx=mem) for k in range(2)]
        k_b = [sb(f"a_kb{k}", [P, 2, T], F32R, ctx=mem) for k in range(2)]
        high = sb("a_high", [P, 2, T], F32R, ctx=mem)
        low = sb("a_low", [P, 2, T], F32R, ctx=mem)
        w_q = sb("a_wq", [P, 2, KC, P], ctx=mem)
        w_k = sb("a_wk", [R, 2, P], ctx=mem)
        vals = sb("a_v", [P, 2, QT, P], ctx=mem)
        prob = sb("a_p", [P, 4, T], ctx=mem)
        scor = sb("a_s", [P, 2, T], ctx=mem)
        probT = sb("a_pT", [P, 2, 2, QT, P], ctx=mem)
        yT = sb("a_yT", [P, 2, T], ctx=mem)
        nmax = sb("a_nmax", [P, 2, UNITS], ctx=mem)
        rsum = sb("a_rsum", [P, 2, UNITS], ctx=mem)
        rinv = sb("a_rinv", [P, 2, UNITS], ctx=mem)
        spot = sb("a_spot", [P, 1], ctx=mem)
        p_s = [ps(f"a_ps{k}", T, mem) for k in range(2)]
        p_t = [ps(f"a_pt{k}", 512, mem) for k in range(2)]
        p_y = ps("a_py", 512, mem)
        p_p = ps("a_pp", 512, mem)
        w_ready = [sem(f"a_w_ready{k}") for k in range(2)]
        v_ready = [sem(f"a_v_ready{k}") for k in range(2)]
        qk_ready = [sem(f"a_qk_ready{k}") for k in range(2)]
        y_out = [sem(f"a_y_out{k}") for k in range(2)]
        projected = sem("a_projected")
        high_done = sem("a_high_done")
        low_done = sem("a_low_done")
        s_done = sem("a_s_done")
        max_done = sem("a_max_done")
        exp_done = sem("a_exp_done")
        inv_done = sem("a_inv_done")
        norm_done = sem("a_norm_done")
        t_done = sem("a_t_done")
        pT_ready = sem("a_pT_ready")
        pv_done = sem("a_pv_done")
        y_copied = sem("a_y_copied")
        QK = 12 * DMA

        def both(eng, body):
            body(0, 0)
            body(1, 1)
            with eng.Fori(1, NP // 2 - 1) as m:
                body(2 * m, 0)
                body(2 * m + 1, 1)
            body(NP - 2, 0)
            body(NP - 1, 1)

        def half(n, k):
            return n // 2 if isinstance(n, int) else (n - k) // 2

        def column(n):
            return (n // PAIRS) * T

        with nc.Block() as block:
            @block.sync
            def _(sp):
                def load_weights(n, k):
                    p = n % PAIRS
                    need(sp, projected, 4 * (n - 1))
                    sp.dma_start(w_q[:, k, :, :], wq[:, ds(p * P, P)].rearrange("(k p) n -> p k n", p=P)).then_inc(w_ready[k], DMA)
                    sp.dma_start(w_k[:, k, :], wku[:, ds(p * P, P)]).then_inc(w_ready[k], DMA)

                def load_values(n, k):
                    p = n % PAIRS
                    need(sp, pv_done, QT * (n - 1))
                    sp.dma_start(vals[:, k, :, :], v_d[ds(column(n), T), ds(p * P, P)].rearrange("(j p) n -> p j n", p=P)).then_inc(v_ready[k], DMA)

                def lay_out(n, k):
                    lo, hi = slice(0, D), slice(D, P)
                    def move(dst, src):
                        sp.dma_start(dst.bitcast(F32), src.bitcast(F32)).then_inc(qk_ready[k], DMA)
                    sp.wait_ge(low_done, 4 * n + 2)
                    move(q_s[k][lo, 0, :], high[lo, 0, :])
                    move(q_s[k][hi, 0, :], low[lo, 0, :])
                    move(q_s[k][hi, 1, :], high[hi, 0, :])
                    move(q_s[k][lo, 1, :], low[hi, 0, :])
                    sp.wait_ge(low_done, 4 * n + 4)
                    move(k_a[k][lo, 0, :], high[lo, 1, :])
                    move(k_a[k][hi, 0, :], low[lo, 1, :])
                    move(k_a[k][hi, 1, :], high[hi, 1, :])
                    move(k_a[k][lo, 1, :], low[hi, 1, :])
                    move(k_b[k][hi, 0, :], high[lo, 1, :])
                    move(k_b[k][lo, 0, :], low[lo, 1, :])
                    move(k_b[k][lo, 1, :], high[hi, 1, :])
                    move(k_b[k][hi, 1, :], low[hi, 1, :])

                def store(n, k):
                    sp.wait_ge(y_copied, QT * (n + 1))
                    sp.dma_start(y_d[ds(n, 1), :, :].rearrange("a p t -> (a p) t"), yT[:, k, :]).then_inc(y_out[k], DMA)

                def body(n, k):
                    last = isinstance(n, int) and n == NP - 1
                    if not last:
                        load_values(n + 1, 1 - k)
                    if not (isinstance(n, int) and n >= NP - 2):
                        load_weights(n + 2, k)
                    if not (isinstance(n, int) and n == 0):
                        store(n - 1, 1 - k)
                    if not last:
                        lay_out(n + 1, 1 - k)

                load_weights(0, 0)
                load_weights(1, 1)
                load_values(0, 0)
                lay_out(0, 0)
                both(sp, body)
                store(NP - 1, 1)
                for k in range(2):
                    sp.wait_ge(y_out[k], DMA * NP // 2)

            @block.tensor
            def _(pe):
                def project(n, k, r):
                    if r == 0:
                        pe.wait_ge(w_ready[k], 2 * DMA * (half(n, k) + 1))
                    need(pe, low_done, 4 * n + r)
                    at = column(n) + 512 * (r % 2)
                    if r < 2:
                        for kc in range(KC):
                            mm = pe.matmul(p_p[:, :], w_q[:, k, kc, :], hT[:, kc, ds(at, 512)],
                                           start=(kc == 0), stop=(kc == KC - 1))
                    else:
                        mm = pe.matmul(p_p[:, :], w_k[:, k, :], latT[:, ds(at, 512)], start=True, stop=True)
                    mm.then_inc(projected, 1)

                def score(n, k, u):
                    i, h = u // 2, u % 2
                    if u == 0:
                        pe.wait_ge(qk_ready[k], QK * (half(n, k) + 1))
                    need(pe, max_done, UNITS * n + u - 1)
                    for at, w in chunks(i):
                        for part, keys in enumerate((k_a[k], k_b[k])):
                            mm = pe.matmul(p_s[h][:, at:at + w], q_s[k][:, h, i * P:(i + 1) * P],
                                           keys[:, h, at:at + w], start=(part == 0), stop=(part == 1))
                    mm.then_inc(s_done, 1)

                def turn(n, u):
                    pe.wait_ge(norm_done, UNITS * n + u + 1)
                    for r in range(ROUNDS[u]):
                        at = FIRST_ROUND[u] + r
                        need(pe, pT_ready, NR * n + at - 1)
                        for j in range(4 * r, min(4 * r + 4, BLOCKS[u])):
                            mm = pe.transpose(p_t[at % 2][:, (j % 4) * P:(j % 4 + 1) * P],
                                              prob[:, u % 4, j * P:(j + 1) * P], ident[:, :])
                        mm.then_inc(t_done, 1)

                def values(n, k, i):
                    if i == 0:
                        pe.wait_ge(v_ready[k], DMA * (half(n, k) + 1))
                    pe.wait_ge(pT_ready, NR * n + FIRST_ROUND[2 * i + 2])
                    need(pe, y_copied, QT * n + i)
                    for j in range(i + 1):
                        for h in range(2):
                            mm = pe.matmul(p_y[h * D:(h + 1) * D, 0:P], vals[:, k, j, h * D:(h + 1) * D],
                                           probT[:, i % 2, h, j, :], start=(j == 0), stop=(j == i),
                                           skip_group_check=True)
                    mm.then_inc(pv_done, 1)

                def body(n, k):
                    first = isinstance(n, int) and n == 0
                    last = isinstance(n, int) and n == NP - 1
                    for u in range(UNITS):
                        score(n, k, u)
                        if u >= LAG:
                            turn(n, u - LAG)
                        elif not first:
                            turn(n - 1, UNITS + u - LAG)
                        if u % 2 == 1:
                            if u >= 5:
                                values(n, k, (u - 5) // 2)
                            elif not first:
                                values(n - 1, 1 - k, QT + (u - 5) // 2)
                        if u in PROJECT_AT and not last:
                            project(n + 1, 1 - k, PROJECT_AT.index(u))

                for r in range(4):
                    project(0, 0, r)
                both(pe, body)
                turn(NP - 1, UNITS - 3)
                turn(NP - 1, UNITS - 2)
                values(NP - 1, 1, QT - 2)
                turn(NP - 1, UNITS - 1)
                values(NP - 1, 1, QT - 1)

            @block.scalar
            def _(act):
                def part_high(n, r):
                    act.wait_ge(projected, 4 * n + r + 1)
                    if r == 0:
                        need(act, qk_ready[1], QK * (n // 2)) if isinstance(n, int) and n % 2 == 0 else None
                    act.copy(high[:, r // 2, (r % 2) * 512:(r % 2 + 1) * 512], p_p[:, :]).then_inc(high_done, 1)

                def exponent(n, k, u):
                    w = BLOCKS[u] * P
                    act.wait_ge(max_done, UNITS * n + u + 1)
                    need(act, t_done, NR * n + FIRST_ROUND[u - 3] if u >= 4 else NR * (n - 1) + FIRST_ROUND[UNITS + u - 3])
                    act.activation(prob[:, u % 4, 0:w], scor[:, u % 2, 0:w], ACT.Exp, scale=-1.0,
                                   bias=nmax[:, k, u:u + 1], accum_out=rsum[:, k, u:u + 1]).then_inc(exp_done, 1)

                def take(n, u):
                    i, h = u // 2, u % 2
                    for r in range(ROUNDS[u]):
                        at = FIRST_ROUND[u] + r
                        act.wait_ge(t_done, NR * n + at + 1)
                        if r == 0:
                            need(act, pv_done, QT * n + i - 1)
                        blocks = min(4, BLOCKS[u] - 4 * r)
                        act.copy(probT[:, i % 2, h, 4 * r:4 * r + blocks, :].rearrange("p j c -> p (j c)"),
                                 p_t[at % 2][:, 0:blocks * P]).then_inc(pT_ready, 1)

                def body(n, k):
                    first = isinstance(n, int) and n == 0
                    last = isinstance(n, int) and n == NP - 1
                    for u in range(UNITS):
                        if u >= LAG:
                            take(n, u - LAG)
                        elif not first:
                            take(n - 1, UNITS + u - LAG)
                        exponent(n, k, u)
                        if u in PROJECT_AT and not last:
                            if u == PROJECT_AT[0]:
                                act.wait_ge(qk_ready[k], QK * (half(n, k) + 1))
                            part_high(n + 1, PROJECT_AT.index(u))

                for r in range(4):
                    part_high(0, r)
                both(act, body)
                take(NP - 1, UNITS - 3)
                take(NP - 1, UNITS - 2)
                take(NP - 1, UNITS - 1)

            @block.vector
            def _(dve):
                def part_low(n, r):
                    dve.wait_ge(high_done, 4 * n + r + 1)
                    col = slice((r % 2) * 512, (r % 2 + 1) * 512)
                    dve.tensor_tensor(low[:, r // 2, col], p_p[:, :], high[:, r // 2, col].bitcast(F32),
                                      ALU.subtract).then_inc(low_done, 1)

                def maximum(n, k, u):
                    i, h = u // 2, u % 2
                    w = BLOCKS[u] * P
                    held(dve, s_done, UNITS * n + u + 1, spot[:, :])
                    dve.tensor_tensor_reduce(out=scor[:, h, 0:w], in0=p_s[h][:, 0:w],
                                             in1=causal[:, T - w:T], scale=-SCALE, scalar=3e38,
                                             op0=ALU.add, op1=ALU.min,
                                             accum_out=nmax[:, k, u:u + 1]).then_inc(max_done, 1)

                def normalise(n, k, u):
                    w = BLOCKS[u] * P
                    dve.wait_ge(exp_done, UNITS * n + u + 1)
                    dve.reciprocal(rinv[:, k, u:u + 1], rsum[:, k, u:u + 1]).then_inc(inv_done, 1)
                    dve.wait_ge(inv_done, UNITS * n + u + 1)
                    dve.tensor_scalar(prob[:, u % 4, 0:w], prob[:, u % 4, 0:w], rinv[:, k, u:u + 1], None,
                                      ALU.mult).then_inc(norm_done, 1)

                def result(n, k, i):
                    dve.wait_ge(pv_done, QT * n + i + 1)
                    if i == 0:
                        need(dve, y_out[k], DMA * half(n, k))
                    dve.tensor_copy(yT[:, k, i * P:(i + 1) * P], p_y[:, 0:P]).then_inc(y_copied, 1)

                def body(n, k):
                    first = isinstance(n, int) and n == 0
                    last = isinstance(n, int) and n == NP - 1
                    for u in range(UNITS):
                        if u >= 2:
                            normalise(n, k, u - 2)
                        elif not first:
                            normalise(n - 1, 1 - k, UNITS + u - 2)
                        maximum(n, k, u)
                        if u % 2 == 0:
                            if u >= 6:
                                result(n, k, u // 2 - 3)
                            elif not first:
                                result(n - 1, 1 - k, QT + u // 2 - 3)
                        if u in PROJECT_AT and not last:
                            if u == PROJECT_AT[0]:
                                dve.wait_ge(qk_ready[k], QK * (half(n, k) + 1))
                            part_low(n + 1, PROJECT_AT.index(u))

                for r in range(4):
                    part_low(0, r)
                both(dve, body)
                normalise(NP - 1, 1, UNITS - 2)
                normalise(NP - 1, 1, UNITS - 1)
                result(NP - 1, 1, QT - 3)
                result(NP - 1, 1, QT - 2)
                result(NP - 1, 1, QT - 1)


def after(nc, sb, ps, sem, xf, y_d, wo, wg, w1, w2, w_all, w_in, x1_d, h2_d, rows_d, ident, mhalf,
          before_me, ones_bf, iota_e, base_e, mod_bc, counts, best, chosen, place):
    with ExitStack() as mem:
        spot = sb("c_spot", [P, 1], ctx=mem)
        spot_p = sb("c_spot_p", [P, 1], ctx=mem)
        w_o = sb("c_wo", [P, PAIRS, C], ctx=mem)
        w_g = sb("c_wg", [P, KC, E], ctx=mem)
        y_t = sb("c_y", [P, 2, PAIRS, 2 * P], ctx=mem)
        xt = sb("c_x", [P, G, C], ctx=mem)
        x1 = sb("c_x1", [P, G, C], ctx=mem)
        xn = sb("c_xn", [P, G, C], ctx=mem)
        h2 = sb("c_h2", [P, G, C], ctx=mem)
        xh = sb("c_xh", [P, G, C], ctx=mem)
        h2T = sb("c_h2T", [P, KC, G * P], ctx=mem)
        st = sb("c_st", [P, 2, G, 6], ctx=mem)
        mv = sb("c_mv", [P, 2, G, 2], ctx=mem)
        ve = sb("c_ve", [P, 2, G], ctx=mem)
        rstd = sb("c_rstd", [P, 2, G], ctx=mem)
        sc = sb("c_sc", [P, G, E], ctx=mem)
        m8 = sb("c_m8", [P, G, 8], ctx=mem)
        i8 = sb("c_i8", [P, G, 8], U32, ctx=mem)
        idf = sb("c_idf", [P, G, TOP], ctx=mem)
        one = sb("c_one", [P, G, TOP, E], ctx=mem)
        mark = sb("c_mark", [P, G, E], BF16, ctx=mem)
        msum = sb("c_msum", [P, E], ctx=mem)
        rank = sb("c_rank", [P, G, E], ctx=mem)
        prod = sb("c_prod", [P, G, TOP, E], ctx=mem)
        pos = sb("c_pos", [P, G, TOP], ctx=mem)
        posu = sb("c_posu", [P, G * TOP], U32, ctx=mem)
        p_o = ps("c_po", G * C, mem)
        p_x = ps("c_px", KC * 512, mem)
        p_r = ps("c_pr", 512, mem)
        p_k = ps("c_pk", 512, mem)
        c_w = sem("c_w")
        y_in = [sem(f"c_y_in{i}") for i in range(2)]
        x_in = sem("c_x_in")
        o_done = sem("c_o_done")
        chain = sem("c_chain")
        var_ready = sem("c_var_ready")
        rstd_ready = sem("c_rstd_ready")
        x1_done = sem("c_x1_done")
        h2_done = sem("c_h2_done")
        x1_out = sem("c_x1_out")
        h2_out = sem("c_h2_out")
        xh_done = sem("c_xh_done")
        hT_done = sem("c_hT_done")
        hT_copied = sem("c_hT_copied")
        r_done = sem("c_r_done")
        mark_done = sem("c_mark_done")
        rank_done = sem("c_rank_done")
        pos_done = sem("c_pos_done")
        sent = sem("c_sent")
        LINKS = 42

        with nc.Block() as block:
            @block.sync
            def _(sp):
                sp.dma_start(w_o[:, :, :], wo.rearrange("(a p) n -> p a n", p=P)).then_inc(c_w, DMA)
                sp.dma_start(w_g[:, :, :], wg.rearrange("(k p) n -> p k n", p=P)).then_inc(c_w, DMA)

                def load(g):
                    b, half = g // GB, g % GB
                    for i in range(2):
                        need(sp, o_done, 2 * g - 1 + i)
                        sp.dma_start(y_t[:, i, :, :], y_d[ds(b * PAIRS, PAIRS), :, ds(half * (G * P) + i * 2 * P, 2 * P)]
                                     .rearrange("a p t -> p a t")).then_inc(y_in[i], DMA)
                    need(sp, x1_done, g)
                    sp.dma_start(xt[:, :, :], xf[ds(g * (G * P), G * P), :].rearrange("(j p) c -> p j c", p=P)).then_inc(x_in, DMA)

                def store(g):
                    sp.wait_ge(x1_done, g + 1)
                    sp.dma_start(x1_d[ds(g * (G * P), G * P), :].rearrange("(j p) c -> p j c", p=P), x1[:, :, :]).then_inc(x1_out, DMA)
                    sp.wait_ge(h2_done, g + 1)
                    sp.dma_start(h2_d[ds(g * (G * P), G * P), :].rearrange("(j p) c -> p j c", p=P), h2[:, :, :]).then_inc(h2_out, DMA)

                def load_expert(e):
                    sp.dma_start(w_all[:, ds(e, 1), 0:KC * F].rearrange("p a (k f) -> p (a k) f", k=KC),
                                 w1[ds(e, 1)].rearrange("a (k p) f -> p (a k) f", p=P)).then_inc(w_in, DMA)
                    sp.dma_start(w_all[:, ds(e, 1), KC * F:].rearrange("p a (k c) -> p (a k) c", k=FC),
                                 w2[ds(e, 1)].rearrange("a (k p) c -> p (a k) c", p=P)).then_inc(w_in, DMA)

                load(0)
                with sp.Fori(0, GROUPS - 1) as g:
                    load(g + 1)
                    load_expert(g)
                    store(g)
                load_expert(GROUPS - 1)
                store(GROUPS - 1)
                sp.wait_ge(x1_out, DMA * GROUPS)
                sp.wait_ge(h2_out, DMA * GROUPS)

            @block.gpsimd
            def _(pool):
                def body(g):
                    for n in range(2):
                        pool.wait_ge(var_ready, 2 * g + n + 1)
                        pool.tensor_tensor(rstd[:, n, :], ve[:, n, :], mhalf[:, :], ALU.pow).then_inc(rstd_ready, 1)
                    pool.wait_ge(pos_done, g + 1)
                    pool.wait_ge(xh_done, g + 1)
                    pool.tensor_tensor(spot_p[:, :], mhalf[:, 0:1], mhalf[:, 0:1], ALU.add)
                    for j in range(G):
                        for t in range(TOP):
                            a = j * TOP + t
                            pool.indirect_dma_start(rows_d[:, :], bass.IndirectOffsetOnAxis(ap=posu[:, a:a + 1], axis=0),
                                                    xh[:, j, :], None).then_inc(sent, DMA)
                rounds(pool, body, GROUPS)
                pool.wait_ge(sent, DMA * TOP * TILES)

            @block.tensor
            def _(pe):
                pe.wait_ge(c_w, 2 * DMA)

                def project(g, tiles):
                    for j in tiles:
                        if j % 2 == 0:
                            pe.wait_ge(y_in[j // 2], DMA * (g + 1))
                        if j == 0:
                            need(pe, x1_done, g)
                        for a in range(PAIRS):
                            mm = pe.matmul(p_o[:, j * C:(j + 1) * C], y_t[:, j // 2, a, (j % 2) * P:(j % 2 + 1) * P],
                                           w_o[:, a, :], start=(a == 0), stop=(a == PAIRS - 1))
                        if j % 2 == 1:
                            mm.then_inc(o_done, 1)

                def body(g):
                    last = isinstance(g, int) and g == GROUPS - 1
                    if not last:
                        project(g + 1, (0, 1))
                    pe.wait_ge(h2_done, g + 1)
                    need(pe, hT_copied, g * KC)
                    for j in range(G):
                        for k in range(KC):
                            mm = pe.transpose(p_x[:, k * 512 + j * P:k * 512 + (j + 1) * P],
                                              h2[:, j, k * P:(k + 1) * P], ident[:, :])
                    mm.then_inc(hT_done, 1)
                    pe.wait_ge(hT_copied, g * KC + KC)
                    for j in range(G):
                        for k in range(KC):
                            mm = pe.matmul(p_r[:, j * E:(j + 1) * E], h2T[:, k, j * P:(j + 1) * P], w_g[:, k, :],
                                           start=(k == 0), stop=(k == KC - 1))
                    mm.then_inc(r_done, 1)
                    if not last:
                        project(g + 1, (2,))
                    pe.wait_ge(mark_done, g + 1)
                    for j in range(G):
                        pe.matmul(p_k[:, j * E:(j + 1) * E], before_me[:, :], mark[:, j, :], start=True, stop=False)
                        for i in range(j):
                            pe.matmul(p_k[:, j * E:(j + 1) * E], ones_bf[:, :], mark[:, i, :], start=False, stop=False)
                        mm = pe.matmul(p_k[:, j * E:(j + 1) * E], ones_bf[:, :], counts[:, :], start=False, stop=True)
                    mm.then_inc(rank_done, 1)
                    if not last:
                        project(g + 1, (3,))

                project(0, range(G))
                rounds(pe, body, GROUPS - 1)
                body(GROUPS - 1)

            @block.scalar
            def _(act):
                def body(g):
                    act.wait_ge(hT_done, g + 1)
                    need(act, r_done, g)
                    for k in range(KC):
                        act.copy(h2T[:, k, :], p_x[:, k * 512:(k + 1) * 512]).then_inc(hT_copied, 1)
                rounds(act, body, GROUPS)

            @block.vector
            def _(dve):
                def body(g):
                    b = g // GB
                    links = Tally(chain, g, LINKS)

                    def link(ins):
                        dve.wait_ge(chain, links.inc(ins))

                    def all_tiles(make, before_plain=True):
                        for j in range(G):
                            at = links.inc(make(j))
                        if before_plain:
                            dve.wait_ge(chain, at)
                        else:
                            held(dve, chain, at, spot[:, :])

                    def rows_of(w):
                        return over(mod_bc[:, ds(b, 1), w, :].rearrange("p a c -> p (a c)"), 1, G)

                    def two(w):
                        return over(mod_bc[:, ds(b, 1), w, :].rearrange("p a c -> p (a c)"), 1, 2)

                    def norm_stats(n, src, eps):
                        all_tiles(lambda j: dve.bn_stats(st[:, n, j, :], src[:, j, :]), False)
                        all_tiles(lambda j: dve.bn_aggr(mv[:, n, j, :], st[:, n, j, :]))
                        dve.tensor_scalar(ve[:, n, :], mv[:, n, :, 1], eps, None, ALU.add).then_inc(var_ready, 1)
                        dve.wait_ge(rstd_ready, 2 * g + n + 1)

                    dve.wait_ge(o_done, 2 * g + 2)
                    dve.wait_ge(x_in, DMA * (g + 1))
                    need(dve, x1_out, DMA * g)
                    for i in range(2):
                        link(dve.tensor_tensor(xn[:, 2 * i:2 * i + 2, :], p_o[:, i * 512:(i + 1) * 512].rearrange("p (j c) -> p j c", c=C),
                                               two(0), ALU.mult))
                    dve.tensor_tensor(x1[:, :, :], xn[:, :, :], xt[:, :, :], ALU.add).then_inc(x1_done, 1)
                    dve.wait_ge(x1_done, g + 1)
                    norm_stats(0, x1, EPS_LN)
                    all_tiles(lambda j: dve.tensor_scalar(xn[:, j, :], x1[:, j, :], mv[:, 0, j, 0:1], rstd[:, 0, j:j + 1],
                                                          ALU.subtract, ALU.mult))
                    need(dve, h2_out, DMA * g)
                    link(dve.tensor_tensor(xn[:, :, :], xn[:, :, :], rows_of(2), ALU.mult))
                    dve.tensor_tensor(h2[:, :, :], xn[:, :, :], rows_of(1), ALU.add).then_inc(h2_done, 1)
                    dve.wait_ge(h2_done, g + 1)
                    norm_stats(1, h2, EPS_FFN)
                    need(dve, sent, DMA * TOP * G * g)
                    for j in range(G):
                        ins = dve.tensor_scalar(xh[:, j, :], h2[:, j, :], mv[:, 1, j, 0:1], rstd[:, 1, j:j + 1],
                                                ALU.subtract, ALU.mult)
                    ins.then_inc(xh_done, 1)
                    dve.wait_ge(r_done, g + 1)
                    held(dve, chain, links.inc(dve.tensor_copy(sc[:, :, :], p_r[:, 0:G * E].rearrange("p (j e) -> p j e", e=E))),
                         spot[:, :])
                    all_tiles(lambda j: dve.max(m8[:, j, :], sc[:, j, :]), False)
                    all_tiles(lambda j: dve.max_index(i8[:, j, :], m8[:, j, :], sc[:, j, :]))
                    links.inc(dve.tensor_copy(best[:, ds(g * G, G), :], m8[:, :, 0:TOP]))
                    link(dve.tensor_copy(idf[:, :, :], i8[:, :, 0:TOP]))
                    link(dve.tensor_tensor(one[:, :, :, :], over(idf[:, :, :], 3, E),
                                           over(over(iota_e, 1, TOP), 1, G), ALU.is_equal))
                    links.inc(dve.tensor_copy(chosen[:, ds(g * G, G), :, :], one[:, :, :, :]))
                    dve.tensor_tensor(mark[:, :, :], one[:, :, 0, :], one[:, :, 1, :], ALU.add).then_inc(mark_done, 1)
                    dve.wait_ge(mark_done, g + 1)
                    link(dve.reduce_sum(msum[:, :], mark[:, :, :].rearrange("p j e -> p e j"), AX_X))
                    dve.wait_ge(rank_done, g + 1)
                    links.inc(dve.tensor_tensor(counts[:, :], counts[:, :], msum[:, :], ALU.add))
                    link(dve.tensor_tensor(rank[:, :, :], p_k[:, 0:G * E].rearrange("p (j e) -> p j e", e=E),
                                           over(base_e, 1, G), ALU.add))
                    link(dve.tensor_tensor(prod[:, :, :, :], one[:, :, :, :], over(rank[:, :, :], 2, TOP), ALU.mult))
                    link(dve.reduce_sum(pos[:, :, :], prod[:, :, :, :], AX_X))
                    links.inc(dve.tensor_copy(place[:, ds(g * G, G), :], pos[:, :, :]))
                    dve.tensor_copy(posu[:, :], pos[:, :, :].rearrange("p j t -> p (j t)")).then_inc(pos_done, 1)
                    assert links.k == LINKS, links.k
                rounds(dve, body, GROUPS)


def plan(nc, sb, ps, sem, rows_d, ones_bf, counts, zeros, base_e, part, iota_t, steps, tri8,
         best, chosen, place, gate, plan_e, plan_r, gather_at):
    with ExitStack() as mem:
        cnt = sb("d_cnt", [P, E], ctx=mem)
        pad = sb("d_pad", [P, E], ctx=mem)
        padu = sb("d_padu", [P, E], U32, ctx=mem)
        more = sb("d_more", [P, E, 32], ctx=mem)
        tl = sb("d_tiles", [P, E], ctx=mem)
        sel = sb("d_sel", [P, E, E], ctx=mem)
        end = sb("d_end", [P, E], ctx=mem)
        start = sb("d_start", [P, E], ctx=mem)
        lim = sb("d_lim", [P, 2], ctx=mem)
        jc = sb("d_jc", [P, ET], ctx=mem)
        ge = sb("d_ge", [P, ET, E - 1], ctx=mem)
        gs = sb("d_gs", [P, ET, E - 1], ctx=mem)
        ex = sb("d_ex", [P, ET], ctx=mem)
        se = sb("d_se", [P, ET], ctx=mem)
        rl = sb("d_rl", [P, ET], ctx=mem)
        rw = sb("d_rw", [P, ET], ctx=mem)
        shift = sb("d_shift", [P, E], ctx=mem)
        moved = sb("d_moved", [P, TILES * TOP, E], ctx=mem)
        by = sb("d_by", [P, TILES * TOP], ctx=mem)
        gap = sb("d_gap", [P, TILES], ctx=mem)
        eg = sb("d_eg", [P, TILES], ctx=mem)
        dn = sb("d_dn", [P, TILES], ctx=mem)
        p_n = ps("d_pn", 512, mem)
        n_done = sem("d_n_done")
        pad_done = sem("d_pad_done")
        padded = sem("d_padded")
        gap_done = sem("d_gap_done")
        eg_done = sem("d_eg_done")
        chain = sem("d_chain")

        with nc.Block() as block:
            @block.tensor
            def _(pe):
                pe.matmul(p_n[:, 0:E], ones_bf[:, :], counts[:, :], start=True, stop=True).then_inc(n_done, 1)

            @block.scalar
            def _(act):
                act.wait_ge(gap_done, 1)
                act.activation(eg[:, :], gap[:, :], ACT.Exp).then_inc(eg_done, 1)

            @block.gpsimd
            def _(pool):
                pool.wait_ge(pad_done, 1)
                for e in range(E):
                    pool.indirect_dma_start(rows_d[:, :], bass.IndirectOffsetOnAxis(ap=padu[:, e:e + 1], axis=0),
                                            zeros[:, :], None).then_inc(padded, DMA)
                pool.wait_ge(padded, DMA * E)

            @block.vector
            def _(dve):
                links = Tally(chain, 0, 99)

                def link(ins):
                    dve.wait_ge(chain, links.inc(ins))

                dve.tensor_tensor(gap[:, :], best[:, :, 1], best[:, :, 0], ALU.subtract).then_inc(gap_done, 1)
                dve.wait_ge(n_done, 1)
                link(dve.tensor_copy(cnt[:, :], p_n[:, 0:E]))
                link(dve.tensor_tensor(pad[:, :], cnt[:, :], base_e, ALU.add))
                dve.tensor_scalar(padu[:, :], pad[:, :], part, None, ALU.add).then_inc(pad_done, 1)
                link(dve.tensor_tensor(more[:, :, :], over(cnt[:, :], 2, 32), over(steps, 1, E), ALU.is_gt))
                link(dve.reduce_sum(tl[:, :], more[:, :, :], AX_X))
                link(dve.tensor_tensor(sel[:, :, :], tri8[:, :, :], over(tl[:, :], 1, E), ALU.mult))
                link(dve.reduce_sum(end[:, :], sel[:, :, :], AX_X))
                link(dve.tensor_tensor(start[:, :], end[:, :], tl[:, :], ALU.subtract))
                link(dve.tensor_scalar(lim[:, 0:1], end[:, E - 1:E], -1.0, None, ALU.add))
                link(dve.tensor_tensor(lim[:, 1:2], lim[:, 0:1], start[:, E - 1:E], ALU.max))
                link(dve.tensor_scalar(jc[:, :], iota_t, lim[:, 1:2], None, ALU.min))
                link(dve.tensor_tensor(ge[:, :, :], over(jc[:, :], 2, E - 1), over(end[:, 0:E - 1], 1, ET), ALU.is_ge))
                link(dve.tensor_tensor(gs[:, :, :], ge[:, :, :], over(tl[:, 0:E - 1], 1, ET), ALU.mult))
                link(dve.reduce_sum(ex[:, :], ge[:, :, :], AX_X))
                link(dve.reduce_sum(se[:, :], gs[:, :, :], AX_X))
                link(dve.tensor_tensor(rl[:, :], jc[:, :], se[:, :], ALU.subtract))
                link(dve.tensor_scalar(rw[:, :], rl[:, :], float(P), None, ALU.mult))
                link(dve.scalar_tensor_tensor(out=rl[:, :], in0=ex[:, :], scalar=float(REGION), in1=rw[:, :],
                                              op0=ALU.mult, op1=ALU.add))
                link(dve.tensor_copy(plan_e[:, :], ex[:, :]))
                link(dve.tensor_copy(plan_r[:, :], rl[:, :]))
                link(dve.scalar_tensor_tensor(out=shift[:, :], in0=start[:, :], scalar=float(P), in1=base_e,
                                              op0=ALU.mult, op1=ALU.subtract))
                link(dve.tensor_tensor(moved[:, :, :], chosen[:, :, :, :].rearrange("p n t e -> p (n t) e"),
                                       over(shift[:, :], 1, TILES * TOP), ALU.mult))
                link(dve.reduce_sum(by[:, :], moved[:, :, :], AX_X))
                link(dve.tensor_tensor(gather_at[:, :], by[:, :], place[:, :, :].rearrange("p n t -> p (n t)"), ALU.add))
                dve.wait_ge(eg_done, 1)
                link(dve.tensor_scalar(dn[:, :], eg[:, :], 1.0, None, ALU.add))
                link(dve.reciprocal(gate[:, :, 0], dn[:, :]))
                link(dve.tensor_tensor(gate[:, :, 1], eg[:, :], gate[:, :, 0], ALU.mult))
                link(dve.tensor_tensor(gate[:, :, 2], gate[:, :, 0], gate[:, :, 1], ALU.add))


def experts(nc, sb, ps, sem, w_all, w_in, rows_d, eo_d, b2, ident, bias1, norm_g, norm_b,
            plan_e, plan_r):
    with ExitStack() as mem:
        xg = sb("e_xg", [P, 2, C], ctx=mem)
        xT = sb("e_xT", [P, KC, P], ctx=mem)
        hr = sb("e_hr", [P, F], ctx=mem)
        hT = sb("e_hT", [P, FC, P], ctx=mem)
        yo = sb("e_yo", [P, 2, C], ctx=mem)
        b2_bc = sb("e_b2", [P, E, C], ctx=mem)
        p_x = ps("e_px", 512, mem)
        p_h = ps("e_ph", F, mem)
        p_t = [ps(f"e_pt{k}", 512, mem) for k in range(2)]
        p_o = ps("e_po", 512, mem)
        b2_in = sem("e_b2_in")
        x_in = [sem(f"e_x_in{k}") for k in range(2)]
        xT_done = sem("e_xT_done")
        xT_ready = sem("e_xT_ready")
        h_done = sem("e_h_done")
        h_copied = sem("e_h_copied")
        hT_done = sem("e_hT_done")
        hT_lo = sem("e_hT_lo")
        hT_hi = sem("e_hT_hi")
        o_done = sem("e_o_done")
        y_done = sem("e_y_done")
        y_out = [sem(f"e_y_out{k}") for k in range(2)]

        def tiles(eng, body):
            body(0, 0)
            body(1, 1)
            with eng.Fori(1, ET // 2) as m:
                body(2 * m, 0)
                body(2 * m + 1, 1)

        def half(j, k):
            return j // 2 if isinstance(j, int) else (j - k) // 2

        with nc.Block() as block:
            @block.sync
            def _(sp):
                sp.dma_start(b2_bc[:, :, :].rearrange("p e c -> p (e c)"),
                             b2.rearrange("e c -> (e c)").partition_broadcast(P)).then_inc(b2_in, DMA)

                def body(j, k):
                    need(sp, xT_done, j - 1)
                    row = sp.value_load(plan_r[0:1, ds(j, 1)], min_val=0, max_val=E * REGION - P)
                    sp.dma_start(xg[:, k, :], rows_d[ds(row, P), :]).then_inc(x_in[k], DMA)
                tiles(sp, body)

            @block.gpsimd
            def _(pool):
                def body(j, k):
                    pool.wait_ge(y_done, j + 1)
                    pool.dma_start(eo_d[ds(j * P, P), :], yo[:, k, :]).then_inc(y_out[k], DMA)
                tiles(pool, body)
                for k in range(2):
                    pool.wait_ge(y_out[k], DMA * ET // 2)

            @block.tensor
            def _(pe):
                pe.wait_ge(w_in, 2 * E * DMA)

                def turn_x(j, k):
                    pe.wait_ge(x_in[k], DMA * (half(j, k) + 1))
                    need(pe, xT_ready, KC * j)
                    for c in range(KC):
                        mm = pe.transpose(p_x[:, c * P:(c + 1) * P], xg[:, k, c * P:(c + 1) * P], ident[:, :])
                    mm.then_inc(xT_done, 1)

                def first(j):
                    e = pe.value_load(plan_e[0:1, ds(j, 1)], min_val=0, max_val=E - 1)
                    pe.wait_ge(xT_ready, KC * (j + 1))
                    need(pe, h_copied, 2 * j)
                    for half_f in range(2):
                        for c in range(KC):
                            mm = pe.matmul(p_h[:, half_f * 512:(half_f + 1) * 512], xT[:, c, :],
                                           w_all[:, ds(e, 1), c * F + half_f * 512:c * F + (half_f + 1) * 512]
                                           .rearrange("p a n -> p (a n)"),
                                           start=(c == 0), stop=(c == KC - 1))
                        mm.then_inc(h_done, 1)

                def turn_h(j):
                    for q in range(2):
                        pe.wait_ge(h_copied, 2 * j + q + 1)
                        need(pe, (hT_lo, hT_hi)[q], 4 * j)
                        for f in range(4):
                            mm = pe.transpose(p_t[q][:, f * P:(f + 1) * P], hr[:, (4 * q + f) * P:(4 * q + f + 1) * P],
                                              ident[:, :])
                        mm.then_inc(hT_done, 1)

                def second(j):
                    e = pe.value_load(plan_e[0:1, ds(j, 1)], min_val=0, max_val=E - 1)
                    pe.wait_ge(hT_lo, 4 * (j + 1))
                    pe.wait_ge(hT_hi, 4 * (j + 1))
                    need(pe, y_done, j)
                    for f in range(FC):
                        mm = pe.matmul(p_o[:, 0:C], hT[:, f, :],
                                       w_all[:, ds(e, 1), KC * F + f * C:KC * F + (f + 1) * C].rearrange("p a n -> p (a n)"),
                                       start=(f == 0), stop=(f == FC - 1))
                    mm.then_inc(o_done, 1)

                turn_x(0, 0)
                first(0)
                turn_x(1, 1)
                turn_h(0)

                def body(j, k):
                    first(j)
                    if not (isinstance(j, int) and j == ET - 1):
                        turn_x(j + 1, 1 - k)
                    second(j - 1)
                    turn_h(j)
                body(1, 1)
                with pe.Fori(1, ET // 2 - 1) as m:
                    body(2 * m, 0)
                    body(2 * m + 1, 1)
                body(ET - 2, 0)
                body(ET - 1, 1)
                second(ET - 1)

            @block.scalar
            def _(act):
                def body(j, k):
                    for q in range(2):
                        act.wait_ge(h_done, 2 * j + q + 1)
                        need(act, hT_done, 2 * (j - 1) + q + 1)
                        act.copy(hr[:, q * 512:(q + 1) * 512], p_h[:, q * 512:(q + 1) * 512]).then_inc(h_copied, 1)
                    e = act.value_load(plan_e[0:1, ds(j, 1)], min_val=0, max_val=E - 1)
                    act.wait_ge(hT_done, 2 * j + 1)
                    need(act, o_done, j)
                    for f in range(4):
                        act.activation(hT[:, f, :], p_t[0][:, f * P:(f + 1) * P], ACT.Relu,
                                       bias=bias1[:, ds(e, 1), f], scale=1.0).then_inc(hT_lo, 1)
                tiles(act, body)

            @block.vector
            def _(dve):
                dve.wait_ge(b2_in, DMA)

                def start_x(j, k):
                    e = dve.value_load(plan_e[0:1, ds(j, 1)], min_val=0, max_val=E - 1)
                    dve.wait_ge(xT_done, j + 1)
                    need(dve, h_done, 2 * j)
                    for c in range(KC):
                        dve.tensor_scalar(xT[:, c, :], p_x[:, c * P:(c + 1) * P], norm_g[:, ds(e, 1), c],
                                          norm_b[:, ds(e, 1), c], ALU.mult, ALU.add).then_inc(xT_ready, 1)

                def finish(j, k):
                    e = dve.value_load(plan_e[0:1, ds(j, 1)], min_val=0, max_val=E - 1)
                    dve.wait_ge(o_done, j + 1)
                    need(dve, y_out[k], DMA * half(j, k))
                    dve.tensor_tensor(yo[:, k, :], p_o[:, 0:C], b2_bc[:, ds(e, 1), :].rearrange("p a c -> p (a c)"),
                                      ALU.add).then_inc(y_done, 1)

                def hidden(j):
                    e = dve.value_load(plan_e[0:1, ds(j, 1)], min_val=0, max_val=E - 1)
                    dve.wait_ge(hT_done, 2 * j + 2)
                    need(dve, o_done, j)
                    for f in range(4):
                        dve.tensor_scalar(hT[:, 4 + f, :], p_t[1][:, f * P:(f + 1) * P], bias1[:, ds(e, 1), 4 + f], 0.0,
                                          ALU.add, ALU.max).then_inc(hT_hi, 1)

                start_x(0, 0)
                start_x(1, 1)
                hidden(0)

                def body(j, k):
                    if not (isinstance(j, int) and j == ET - 1):
                        start_x(j + 1, 1 - k)
                    finish(j - 1, 1 - k)
                    hidden(j)
                body(1, 1)
                with dve.Fori(1, ET // 2 - 1) as m:
                    body(2 * m, 0)
                    body(2 * m + 1, 1)
                body(ET - 2, 0)
                body(ET - 1, 1)
                finish(ET - 1, 1)


def combine(nc, sb, sem, eo_d, x1_d, h2_d, outf, mod_bc, gate, gather_at):
    with ExitStack() as mem:
        spot_p = sb("f_spot_p", [P, 1], ctx=mem)
        at_now = sb("f_at", [P, 2, G * TOP], U32, ctx=mem)
        rows = sb("f_rows", [P, 2, G, TOP, C], ctx=mem)
        x1 = sb("f_x1", [P, 2, G, C], ctx=mem)
        h2 = sb("f_h2", [P, 2, G, C], ctx=mem)
        acc = sb("f_acc", [P, G, C], ctx=mem)
        res = sb("f_res", [P, 2, G, C], ctx=mem)
        carried = sem("f_carried")
        at_ready = sem("f_at_ready")
        rows_in = [sem(f"f_rows_in{k}") for k in range(2)]
        x_in = [sem(f"f_x_in{k}") for k in range(2)]
        chain = sem("f_chain")
        res_done = sem("f_res_done")
        stored = [sem(f"f_stored{k}") for k in range(2)]
        LINKS = 3 * G + 1

        def groups(eng, body):
            body(0, 0)
            body(1, 1)
            with eng.Fori(1, GROUPS // 2) as m:
                body(2 * m, 0)
                body(2 * m + 1, 1)

        def half(g, k):
            return g // 2 if isinstance(g, int) else (g - k) // 2

        with nc.Block() as block:
            @block.gpsimd
            def _(pool):
                def body(g, k):
                    pool.wait_ge(at_ready, g + 1)
                    need(pool, res_done, g - 1)
                    need(pool, carried, g)
                    pool.tensor_tensor(spot_p[:, :], gate[:, 0, 0:1], gate[:, 0, 0:1], ALU.add).then_inc(carried, 1)
                    for j in range(G):
                        for t in range(TOP):
                            a = j * TOP + t
                            pool.indirect_dma_start(rows[:, k, j, t, :], None, eo_d[:, :],
                                                    bass.IndirectOffsetOnAxis(ap=at_now[:, k, a:a + 1], axis=0)).then_inc(rows_in[k], DMA)
                groups(pool, body)

            @block.sync
            def _(sp):
                def tokens(g):
                    return ds(g * (G * P), G * P)

                def body(g, k):
                    need(sp, res_done, g - 1)
                    sp.dma_start(x1[:, k, :, :], x1_d[tokens(g), :].rearrange("(j p) c -> p j c", p=P)).then_inc(x_in[k], DMA)
                    sp.dma_start(h2[:, k, :, :], h2_d[tokens(g), :].rearrange("(j p) c -> p j c", p=P)).then_inc(x_in[k], DMA)
                groups(sp, body)

            @block.scalar
            def _(act):
                def body(g, k):
                    act.wait_ge(res_done, g + 1)
                    act.dma_start(outf[ds(g * (G * P), G * P), :].rearrange("(j p) c -> p j c", p=P), res[:, k, :, :]).then_inc(stored[k], DMA)
                groups(act, body)
                for k in range(2):
                    act.wait_ge(stored[k], DMA * GROUPS // 2)

            @block.vector
            def _(dve):
                def where(g, k):
                    need(dve, rows_in[k], DMA * G * TOP * half(g, k))
                    dve.tensor_copy(at_now[:, k, :], gather_at[:, ds(g * (G * TOP), G * TOP)]).then_inc(at_ready, 1)

                def body(g, k):
                    b = g // GB
                    if not (isinstance(g, int) and g >= GROUPS - 1):
                        where(g + 1, 1 - k)
                    dve.wait_ge(rows_in[k], DMA * G * TOP * (half(g, k) + 1))
                    dve.wait_ge(x_in[k], 2 * DMA * (half(g, k) + 1))
                    need(dve, stored[k], DMA * half(g, k))
                    need(dve, res_done, g)
                    links = Tally(chain, g, LINKS)
                    for j in range(G):
                        at = links.inc(dve.tensor_scalar(acc[:, j, :], rows[:, k, j, 0, :], gate[:, ds(g * G + j, 1), 0], None, ALU.mult))
                    dve.wait_ge(chain, at)
                    for j in range(G):
                        at = links.inc(dve.scalar_tensor_tensor(out=acc[:, j, :], in0=rows[:, k, j, 1, :],
                                                                scalar=gate[:, ds(g * G + j, 1), 1], in1=acc[:, j, :],
                                                                op0=ALU.mult, op1=ALU.add))
                    dve.wait_ge(chain, at)
                    for j in range(G):
                        at = links.inc(dve.scalar_tensor_tensor(out=acc[:, j, :], in0=h2[:, k, j, :],
                                                                scalar=gate[:, ds(g * G + j, 1), 2], in1=acc[:, j, :],
                                                                op0=ALU.mult, op1=ALU.add))
                    dve.wait_ge(chain, at)
                    gb = over(mod_bc[:, ds(b, 1), 3, :].rearrange("p a c -> p (a c)"), 1, G)
                    dve.wait_ge(chain, links.inc(dve.tensor_tensor(acc[:, :, :], acc[:, :, :], gb, ALU.mult)))
                    dve.tensor_tensor(res[:, k, :, :], acc[:, :, :], x1[:, k, :, :], ALU.add).then_inc(res_done, 1)

                where(0, 0)
                body(0, 0)
                body(1, 1)
                with dve.Fori(1, GROUPS // 2 - 1) as m:
                    body(2 * m, 0)
                    body(2 * m + 1, 1)
                body(GROUPS - 2, 0)
                body(GROUPS - 1, 1)


_INS = ['L0_attn_x', 'L0_attn_w_kv_down', 'L0_attn_w_kv_up', 'L0_attn_w_q', 'L0_attn_w_out', 'L0_ffn_Wg',
        'L0_ffn_gamma', 'L0_ffn_beta', 'L0_ffn_W1', 'L0_ffn_b1', 'L0_ffn_W2', 'L0_ffn_b2', 'L0_c', 'L0_wmod']
_OUTS = [((B, T, C), 'float32')]


def kernel(**inputs):
    import numpy as _np
    import concourse.bacc as _bacc
    from concourse import mybir as _mybir
    from concourse.bass_utils import run_bass_kernel_spmd as _run

    nc = _bacc.Bacc("TRN2", target_bir_lowering=False, num_devices=1)
    arrays, args = {}, []
    for name in _INS:
        a = _np.ascontiguousarray(inputs[name])
        arrays[f"in_{name}_dram"] = a
        args.append(nc.dram_tensor(f"in_{name}_dram", a.shape, _mybir.dt.from_np(a.dtype), kind="ExternalInput").ap())
    for i, (shape, dtype) in enumerate(_OUTS):
        dt = _mybir.dt.from_np(_np.dtype(dtype))
        args.append(nc.dram_tensor(f"out_{i}_dram", shape, dt, kind="ExternalOutput").ap())
    block_kernel(nc, *args)
    r = _run(nc, [arrays], core_ids=[0])
    got = tuple(r.results[0][f"out_{i}_dram"] for i in range(len(_OUTS)))
    return got[0]
```
